# Optimizing a Trainium2 kernel written in Bass

```python
import numpy as np
import jax
import jax.numpy as jnp

def _softmax(x, axis=-1):
    return jax.nn.softmax(x, axis=axis)

def _gelu(x):
    return jax.nn.gelu(x, approximate=True)

def _silu(x):
    return jax.nn.silu(x)

def _sigmoid(x):
    return jax.nn.sigmoid(x)

def _layernorm(x, axis=-1, eps=1e-05):
    m = jnp.mean(x, axis=axis, keepdims=True)
    v = jnp.var(x, axis=axis, keepdims=True)
    return (x - m) / jnp.sqrt(v + eps)

def _scatter_add(tgt, idx, src, axis=0):
    return tgt.at[idx].add(src)

def _segment_sum(src, seg, n):
    return jax.ops.segment_sum(src, seg, n)
kernel_name = 'mk_gps_d1_gnn_r8_cbff3d'

def setup_inputs(seed: int=0):
    np.random.seed(seed)
    _w = jnp.asarray

    def _rec_inputs():
        import jax
        import jax.numpy as jnp
        _gk = jax.random.key(seed)
        x = -0.0003713 + 1 * jax.random.normal(jax.random.fold_in(_gk, 1), (6250, 256), jnp.float32)
        _s = jax.random.randint(jax.random.fold_in(_gk, 2), (100000,), 0, 6250, jnp.int32)
        _d = jax.random.randint(jax.random.fold_in(_gk, 3), (100000,), 0, 6250, jnp.int32)
        _loop = jnp.arange(6250, dtype=jnp.int32)
        src = jnp.concatenate([_s, _d, _loop])
        dst = jnp.concatenate([_d, _s, _loop])
        _o = jnp.argsort(dst, stable=True)
        src = src[_o]
        dst = dst[_o]
        return (x, src, dst)
    x, src, dst = _rec_inputs()

    def _L0_gnn_setup():
        import jax, jax.numpy as jnp
        import numpy as np
        N = 6250
        E = 50000
        IN_CH = 256
        HEADS = 4
        OUT_CH = 64
        HID = HEADS * OUT_CH
        ALPHA = 0.2
        LN_EPS = 1e-05
        key = jax.random.key(seed)
        ks = jax.random.split(key, 8)
        h = jax.random.normal(ks[0], (N, IN_CH), dtype=jnp.float32)
        edge_row = jax.random.randint(ks[1], (E,), 0, N, dtype=jnp.int32)
        edge_col = jax.random.randint(ks[2], (E,), 0, N, dtype=jnp.int32)

        def xavier(k, shape, fan_in, fan_out):
            lim = np.sqrt(6.0 / (fan_in + fan_out)).astype(np.float32)
            return jax.random.uniform(k, shape, jnp.float32, -lim, lim)
        W = xavier(ks[3], (IN_CH, HID), IN_CH, HID)
        attn_fc = xavier(ks[4], (HEADS, 2 * OUT_CH), 2 * OUT_CH, 1)
        ln_gamma = jnp.ones((HID,), jnp.float32)
        ln_beta = jnp.zeros((HID,), jnp.float32)
        ffn_w = xavier(ks[5], (HID, HID), HID, HID)
        ffn_b = jnp.zeros((HID,), jnp.float32)
        return {'h': h, 'edge_row': edge_row, 'edge_col': edge_col, 'W': W, 'attn_fc': attn_fc, 'ln_gamma': ln_gamma, 'ln_beta': ln_beta, 'ffn_w': ffn_w, 'ffn_b': ffn_b}
    _L0_gnn_all = _L0_gnn_setup()
    _L0_gnn_in = {k: v for k, v in _L0_gnn_all.items() if k in ('W', 'attn_fc', 'ln_gamma', 'ln_beta', 'ffn_w', 'ffn_b')}
    del _L0_gnn_all

    def _L0_mix_setup():
        import jax, jax.numpy as jnp
        import numpy as np
        HEADS = 4
        DIM_HEAD = 32
        key = jax.random.key(seed)
        k1, k2, k3 = jax.random.split(key, 3)
        B, L, D = (16, 1024, 256)
        hidden = HEADS * DIM_HEAD
        x = jax.random.normal(k1, (B, L, D), dtype=jnp.float32)
        W_qkv = jax.random.normal(k2, (D, 3 * hidden), dtype=jnp.float32) * D ** (-0.5)
        W_out = jax.random.normal(k3, (hidden, D), dtype=jnp.float32) * hidden ** (-0.5)
        b_out = jnp.zeros((D,), dtype=jnp.float32)
        return {'x': x, 'W_qkv': W_qkv, 'W_out': W_out, 'b_out': b_out}
    _L0_mix_all = _L0_mix_setup()
    _L0_mix_in = {k: v for k, v in _L0_mix_all.items() if k in ('W_qkv', 'W_out', 'b_out')}
    del _L0_mix_all

    def _L0_ffn_setup():
        import jax, jax.numpy as jnp
        import numpy as np
        C = 256
        HID = 1024
        E = 8
        TEMP = 1.0
        key = jax.random.key(seed)
        ks = jax.random.split(key, 7)
        x = jax.random.normal(ks[0], (8, 2048, C), dtype=jnp.float32)
        W1 = jax.random.normal(ks[1], (C, HID), dtype=jnp.float32) * 0.02
        b1 = jnp.zeros((HID,), dtype=jnp.float32)
        Wg = jax.random.normal(ks[2], (HID, E), dtype=jnp.float32) * 0.02
        bg = jnp.zeros((E,), dtype=jnp.float32)
        Wd = jax.random.normal(ks[3], (E, HID, C), dtype=jnp.float32) * 0.02
        bd = jnp.zeros((E, C), dtype=jnp.float32)
        return {'x': x, 'W1': W1, 'b1': b1, 'Wg': Wg, 'bg': bg, 'Wd': Wd, 'bd': bd}
    _L0_ffn_all = _L0_ffn_setup()
    _L0_ffn_in = {k: v for k, v in _L0_ffn_all.items() if k in ('W1', 'b1', 'Wg', 'bg', 'Wd', 'bd')}
    del _L0_ffn_all
    return {'x': x, 'src': src, 'dst': dst, 'L0_gnn_W': _L0_gnn_in['W'], 'L0_gnn_attn_fc': _L0_gnn_in['attn_fc'], 'L0_gnn_ln_gamma': _L0_gnn_in['ln_gamma'], 'L0_gnn_ln_beta': _L0_gnn_in['ln_beta'], 'L0_gnn_ffn_w': _L0_gnn_in['ffn_w'], 'L0_gnn_ffn_b': _L0_gnn_in['ffn_b'], 'L0_mix_W_qkv': _L0_mix_in['W_qkv'], 'L0_mix_W_out': _L0_mix_in['W_out'], 'L0_mix_b_out': _L0_mix_in['b_out'], 'L0_ffn_W1': _L0_ffn_in['W1'], 'L0_ffn_b1': _L0_ffn_in['b1'], 'L0_ffn_Wg': _L0_ffn_in['Wg'], 'L0_ffn_bg': _L0_ffn_in['bg'], 'L0_ffn_Wd': _L0_ffn_in['Wd'], 'L0_ffn_bd': _L0_ffn_in['bd']}

def reference(x, src, dst, L0_gnn_W, L0_gnn_attn_fc, L0_gnn_ln_gamma, L0_gnn_ln_beta, L0_gnn_ffn_w, L0_gnn_ffn_b, L0_mix_W_qkv, L0_mix_W_out, L0_mix_b_out, L0_ffn_W1, L0_ffn_b1, L0_ffn_Wg, L0_ffn_bg, L0_ffn_Wd, L0_ffn_bd):
    import jax
    import jax.numpy as jnp

    def _L0_gnn_ref(h, edge_row, edge_col, W, attn_fc, ln_gamma, ln_beta, ffn_w, ffn_b):
        import jax, jax.numpy as jnp
        import numpy as np
        N = 6250
        E = 50000
        IN_CH = 256
        HEADS = 4
        OUT_CH = 64
        HID = HEADS * OUT_CH
        ALPHA = 0.2
        LN_EPS = 1e-05
        Wh = (h @ W).reshape(N, HEADS, OUT_CH)
        Wh_i = Wh[edge_row]
        Wh_j = Wh[edge_col]
        a_src = attn_fc[:, :OUT_CH]
        a_dst = attn_fc[:, OUT_CH:]
        e = jnp.einsum('ehd,hd->eh', Wh_i, a_src) + jnp.einsum('ehd,hd->eh', Wh_j, a_dst)
        e = jax.nn.leaky_relu(e, negative_slope=ALPHA)
        e = jnp.exp(e - jnp.max(e, axis=0, keepdims=True))
        e_sum = jax.ops.segment_sum(e, edge_row, num_segments=N)
        alpha = e / (e_sum[edge_row] + 1e-15)
        h_new = jax.ops.segment_sum(Wh_j * alpha[..., None], edge_row, num_segments=N)
        h_new = h_new.reshape(N, HID) + Wh.reshape(N, HID)
        mu = jnp.mean(h_new, axis=-1, keepdims=True)
        var = jnp.var(h_new, axis=-1, keepdims=True)
        h_new = (h_new - mu) * jax.lax.rsqrt(var + LN_EPS) * ln_gamma + ln_beta
        return jax.nn.relu(h_new @ ffn_w + ffn_b)

    def _L0_mix_ref(x, W_qkv, W_out, b_out):
        import jax, jax.numpy as jnp
        import numpy as np
        HEADS = 4
        DIM_HEAD = 32
        B, L, D = x.shape
        scale = DIM_HEAD ** (-0.5)
        qkv = jnp.einsum('bld,df->blf', x, W_qkv)
        qkv = qkv.reshape(B, L, 3, HEADS, DIM_HEAD)
        q = jnp.transpose(qkv[:, :, 0], (0, 2, 1, 3)) * scale
        k = jax.nn.softmax(jnp.transpose(qkv[:, :, 1], (0, 2, 1, 3)), axis=2)
        v = jnp.transpose(qkv[:, :, 2], (0, 2, 1, 3))
        context = jnp.einsum('bhld,bhle->bhde', k, v)
        out = jnp.einsum('bhde,bhld->bhle', context, q)
        out = jnp.transpose(out, (0, 2, 1, 3)).reshape(B, L, HEADS * DIM_HEAD)
        return jnp.einsum('blf,fd->bld', out, W_out) + b_out

    def _L0_ffn_ref(x, W1, b1, Wg, bg, Wd, bd):
        import jax, jax.numpy as jnp
        import numpy as np
        C = 256
        HID = 1024
        E = 8
        TEMP = 1.0
        orig_shape = x.shape
        xf = x.reshape(-1, orig_shape[-1])
        H = jax.nn.gelu(xf @ W1 + b1, approximate=False)
        probs = jax.nn.softmax((H @ Wg + bg) / TEMP, axis=-1)
        assign = jnp.argmax(probs, axis=-1)
        out = jnp.zeros_like(xf)
        for e in range(Wd.shape[0]):
            y = H @ Wd[e] + bd[e]
            sel = (assign == e)[:, None]
            out = out + jnp.where(sel, probs[:, e:e + 1] * y, 0.0)
        return out.reshape(orig_shape)
    xn = _layernorm(x, axis=-1)
    x = x + _L0_gnn_ref(xn, src, dst, L0_gnn_W, L0_gnn_attn_fc, L0_gnn_ln_gamma, L0_gnn_ln_beta, L0_gnn_ffn_w, L0_gnn_ffn_b) + _L0_mix_ref(xn[None], L0_mix_W_qkv, L0_mix_W_out, L0_mix_b_out)[0]
    x = x + _L0_ffn_ref(_layernorm(x, axis=-1)[None], L0_ffn_W1, L0_ffn_b1, L0_ffn_Wg, L0_ffn_bg, L0_ffn_Wd, L0_ffn_bd)[0]
    return x

_drawn_inputs = setup_inputs


def setup_inputs(seed=0):
    import zlib

    import numpy as np

    out = dict(_drawn_inputs(seed))
    spreads = {'L0_gnn_ln_gamma': (1.0, 0.2),
     'L0_gnn_ln_beta': (0.0, 0.1),
     'L0_gnn_ffn_b': (0.0, 0.1),
     'L0_mix_b_out': (0.0, 0.1),
     'L0_ffn_b1': (0.0, 0.696),
     'L0_ffn_bg': (0.0, 0.491),
     'L0_ffn_bd': (0.0, 0.69)}
    factors = {'L0_ffn_W1': 3.238, 'L0_ffn_Wg': 3.486, 'L0_ffn_Wd': 3.986}
    for name, (base, spread) in spreads.items():
        noise = np.random.default_rng([zlib.crc32(name.encode()), seed]).standard_normal(out[name].shape)
        drawn = base * np.exp(spread * noise) if base else spread * noise
        out[name] = jnp.asarray(drawn.astype(out[name].dtype))
    for name, factor in factors.items():
        out[name] = (out[name] * factor).astype(out[name].dtype)
    return out
```

```python
from contextlib import ExitStack

import numpy as np

import concourse.bass as bass
from concourse import mybir

F32 = mybir.dt.float32
I32 = mybir.dt.int32
ALU = mybir.AluOpType
ACT = mybir.ActivationFunctionType
AX = mybir.AxisListType

P = 128
N = 6250
C = 256
NB = (N + P - 1) // P
LAST = N - (NB - 1) * P
E = 206250
H, HD = 4, 64
MIX = 128
MH, MD = 4, 32
HID, NE = 1024, 8
EPS = 1e-5

EP, EF = 125, 1650
SORT_BITS = 18
FREE_BITS = 11
FREE = 1 << FREE_BITS
COL_BITS = 13
COL_MASK = (1 << COL_BITS) - 1
FLOAT_BIT = 1 << 30
TILES = 4
GROUP = TILES * P
NG = (E + GROUP - 1) // GROUP
NG += NG % 2
TW = C + H
PRE_FIRST = 25
PRE_GAP = 4


def filler_key():
    return float(np.array([FLOAT_BIT | (COL_MASK << COL_BITS) | N], np.uint32).view(np.float32)[0])


def blocks(nc, eng, start, end, body):
    b = start
    while b < end and (b < 2 or b % 2):
        body(b, b % 2)
        b += 1
    pairs = (end - b) // 2
    if pairs > 1:
        with nc.Fori(b // 2, b // 2 + pairs, engines=[eng.engine]) as i:
            body(2 * i, 0)
            body(2 * i + 1, 1)
        b += 2 * pairs
    while b < end:
        body(b, b % 2)
        b += 1


class Tiles:
    pass


class Count:

    def __init__(self, eng, sem):
        self.eng, self.sem, self.n = eng, sem, 0

    def mark(self, ins):
        ins.then_inc(self.sem, 1)
        self.n += 1
        return self.n

    def settle(self):
        self.eng.wait_ge(self.sem, self.n)

    def then(self, ins):
        self.mark(ins)
        self.settle()


def first_or(b, n):
    return isinstance(b, int) and b < n


def moments(eng, c, st, tmp, mean2, var):
    c.mark(eng.tensor_tensor(mean2, st[:, :, 1], st[:, :, 4], ALU.add))
    c.then(eng.tensor_tensor(tmp[:, 0, :], st[:, :, 1], st[:, :, 4], ALU.subtract))
    c.mark(eng.tensor_tensor(tmp[:, 1, :], tmp[:, 0, :], tmp[:, 0, :], ALU.mult))
    c.then(eng.tensor_tensor(tmp[:, 2, :], st[:, :, 2], st[:, :, 5], ALU.add))
    c.then(eng.scalar_tensor_tensor(tmp[:, 3, :], tmp[:, 1, :], C / 4.0, tmp[:, 2, :], ALU.mult, ALU.add))
    c.then(eng.tensor_scalar(var, tmp[:, 3, :], 1.0 / C, EPS, ALU.mult, ALU.add))


def sort_and_project(nc, io, t):
    ctx = ExitStack()
    with ctx:
        sb = lambda name, shape, dt=F32: ctx.enter_context(nc.sbuf_tensor(name, shape, dt))
        pb = lambda name, shape: ctx.enter_context(nc.psum_tensor(name, shape, F32))
        sem = lambda name: ctx.enter_context(nc.semaphore(name))

        keys = [sb("keys0", [P, FREE], I32), sb("keys1", [P, FREE], I32)]
        src = sb("src_sb", [EP, EF], I32)
        dst = sb("dst_sb", [EP, EF], I32)
        sign_out = sb("sign_out", [EP, EF], mybir.dt.bfloat16)
        sign_sum = sb("sign_sum", [P, NB - 1])
        below = sb("below", [P, NB - 1])
        starts = sb("starts", [NB - 1, 1])
        group_pos = sb("group_pos", [NB - 1, NG + 1])
        lane_i = sb("lane_i", [P, P], I32)
        lane_p = sb("lane_p", [P, 2], I32)
        bits = sb("bits", [P, 8, P], I32)
        flips = sb("flips", [P, 7, P])
        flip0 = sb("flip0", [P, 1])
        stats = sb("stats", [P, NB, 6])
        tmp = sb("tmp", [P, 4, NB])
        mean2 = sb("mean2", [P, NB])
        var = sb("var", [P, NB])
        std = sb("std", [P, NB])
        rstd = sb("rstd", [P, NB])
        shift = sb("shift", [P, NB])
        normed = [sb("normed0", [P, C]), sb("normed1", [P, C])]
        normed_t = [sb("normed_t0", [P, 2, P]), sb("normed_t1", [P, 2, P])]
        rows = [sb("rows0", [P, TW]), sb("rows1", [P, TW])]
        w_all = sb("w_all", [P, 2, TW + H])
        w_t = sb("w_t", [P, 2, C])
        attn = sb("attn", [P, 2, 2 * H])
        w_kv = sb("w_kv", [P, 2, 2 * MIX])
        filler = sb("filler", [1, TW])
        dmax = sb("dmax", [P, 3 * H])
        dmax_col = sb("dmax_col", [H, 1])
        dmax_diag = sb("dmax_diag", [H, H])
        u = sb("u", [P, NB, H])

        swap = [pb(f"swap{q}", [P, 512]) for q in range(4)]
        ps_t = pb("ps_t", [P, 512])
        ps_wh = pb("ps_wh", [P, 512])
        ps_kv = pb("ps_kv", [P, 512])
        ps_m = pb("ps_m", [P, 512])

        edges_in = sem("edges_in")
        weights_in = sem("weights_in")
        x_in = [sem(f"x_in{c}") for c in range(7)]
        made = sem("made")
        dve = sem("dve")
        rooted = sem("rooted")
        signs = sem("signs")
        swapped = sem("swapped")
        w_t_done = sem("w_t_done")
        w_t_out = sem("w_t_out")
        attn_done = sem("attn_done")
        attn_out = sem("attn_out")
        normed_done = sem("normed_done")
        t_done = sem("t_done")
        t_out = sem("t_out")
        proj_done = sem("proj_done")
        proj_out = sem("proj_out")
        t_stored = [sem("t_stored0"), sem("t_stored1")]
        rows_stored = [sem("rows_stored0"), sem("rows_stored1")]
        filler_in = sem("filler_in")
        counts_done = sem("counts_done")
        dmax_done = sem("dmax_done")

        kf = [k[:, :].bitcast(F32) for k in keys]
        block = ctx.enter_context(nc.Block())

        @block.vector
        def _(eng):
            c = Count(eng, dve)
            for q in range(7):
                eng.wait_ge(x_in[q], 16 if q < 6 else 32)
                with nc.Fori(7 * q, 7 * q + 7, engines=[eng.engine]) as b:
                    eng.bn_stats(stats[:, bass.ds(b, 1), :].rearrange("p o c -> p (o c)"),
                                 t.acc[:, bass.ds(b, 1), 0:C].rearrange("p o c -> p (o c)")).then_inc(dve, 1)
                c.n += 7
            c.settle()
            moments(eng, c, stats, tmp, mean2[:, :], var[:, :])
            t.n_moments = c.n
            eng.wait_ge(edges_in, 32)
            eng.wait_ge(made, 7)
            k0 = keys[0][0:EP, 0:EF]
            c.then(eng.tensor_scalar(k0, src[:, :], COL_BITS, FLOAT_BIT, ALU.logical_shift_left, ALU.bitwise_or))
            c.then(eng.tensor_tensor(k0, k0, dst[:, :], ALU.bitwise_or))
            eng.wait_ge(rooted, 1)
            c.then(eng.reciprocal(rstd[:, :], std[:, :]))
            c.then(eng.scalar_tensor_tensor(shift[:, :], mean2[:, :], -0.5, rstd[:, :], ALU.mult, ALU.mult))
            t.n_norms = c.n
            for m in range(7):
                c.mark(eng.tensor_scalar(bits[:, m, :], lane_i[:, :], m, 1, ALU.logical_shift_right,
                                         ALU.bitwise_and))
            c.mark(eng.memset(bits[:, 7, :], 0))
            c.mark(eng.tensor_scalar(lane_p[:, 1:2], lane_p[:, 0:1], 1, None, ALU.bitwise_and))
            c.settle()
            c.then(eng.tensor_tensor(bits[:, 0:7, :], bits[:, 0:7, :], bits[:, 1:8, :], ALU.bitwise_xor))
            c.mark(eng.tensor_scalar(flips[:, :, :], bits[:, 0:7, :], -2.0, 1.0, ALU.mult, ALU.add))
            c.then(eng.tensor_scalar(flip0[:, :], lane_p[:, 1:2], -2.0, 1.0, ALU.mult, ALU.add))

            at = 0

            def stage(j, level=None):
                nonlocal at
                a, o = kf[at], kf[1 - at]
                w = 1 << j
                if level is None:
                    av = a.rearrange("p (a two w) -> p a two w", two=2, w=w)
                    ov = o.rearrange("p (a two w) -> p a two w", two=2, w=w)
                    lo, hi = av[:, :, 0, :], av[:, :, 1, :]
                    c.mark(eng.tensor_tensor(ov[:, :, 0, :], lo, hi, ALU.min))
                    c.mark(eng.tensor_tensor(ov[:, :, 1, :], lo, hi, ALU.max))
                else:
                    h = 1 << (level - j - 1)
                    av = a.rearrange("p (b d a two w) -> p b d a two w", d=2, a=h, two=2, w=w)
                    ov = o.rearrange("p (b d a two w) -> p b d a two w", d=2, a=h, two=2, w=w)
                    for d in range(2):
                        lo, hi = av[:, :, d, :, 0, :], av[:, :, d, :, 1, :]
                        c.mark(eng.tensor_tensor(ov[:, :, d, :, 0, :], lo, hi, ALU.max if d else ALU.min))
                        c.mark(eng.tensor_tensor(ov[:, :, d, :, 1, :], lo, hi, ALU.min if d else ALU.max))
                c.settle()
                at = 1 - at

            for level in range(1, FREE_BITS):
                for j in reversed(range(level)):
                    stage(j, level)
            c.then(eng.tensor_scalar(kf[1 - at], kf[at], flip0[:, 0:1], None, ALU.mult))
            at = 1 - at
            for j in reversed(range(FREE_BITS)):
                stage(j)
            t.swap_after, t.swap_from = [], []

            def exchange(n, evacuate):
                nonlocal at
                t.swap_after.append(c.n)
                t.swap_from.append(at)
                for q in range(4):
                    eng.wait_ge(swapped, 4 * n + q + 1)
                    c.mark(evacuate(kf[1 - at], q))
                c.settle()
                at = 1 - at

            for m in range(1, 8):
                exchange(2 * m - 2, lambda o, q: eng.tensor_tensor(
                    o[:, 512 * q:512 * (q + 1)].rearrange("p (s c) -> p s c", c=P),
                    swap[q][:, :].rearrange("p (s c) -> p s c", c=P),
                    flips[:, m - 1:m, :].to_broadcast([P, 4, P]), ALU.mult))
                for j in reversed(range(m)):
                    stage(j)
                exchange(2 * m - 1, lambda o, q: eng.tensor_copy(o[:, 512 * q:512 * (q + 1)], swap[q][:, :]))
                for j in reversed(range(FREE_BITS)):
                    stage(j)
            exchange(14, lambda o, q: eng.tensor_copy(
                o.rearrange("c (p s) -> c s p", s=16)[:, 4 * q:4 * (q + 1), :],
                swap[q][:, :].rearrange("p (s c) -> p s c", c=P)))
            k, other = keys[at], keys[1 - at]
            c.mark(eng.tensor_scalar(t.edge_col[:, :], k[:, :], COL_MASK, None, ALU.bitwise_and))
            c.then(eng.tensor_scalar(other[:, :], k[:, :], COL_BITS, COL_MASK, ALU.logical_shift_right,
                                     ALU.bitwise_and))
            c.mark(eng.tensor_copy(t.edge_row[:, :], other[:, :]))
            eng.wait_ge(counts_done, 1)
            c.then(eng.tensor_scalar(starts[:, :], ps_m[0:NB - 1, 0:1], 0.5, E / 2.0, ALU.mult, ALU.add))
            c.then(eng.tensor_scalar(group_pos[:, :], group_pos[:, :], starts[:, 0:1], None, ALU.is_ge))
            c.then(eng.memset(group_pos[:, 0:1], 0.0))
            t.n_cmp = c.n
            eng.wait_ge(counts_done, 2)
            c.mark(eng.tensor_copy(t.first_block[:, :], ps_wh[0:1, 0:NG + 1]))
            eng.wait_ge(proj_out, 3 * NB)
            c.then(eng.tensor_reduce(t.k_max[:, :], t.kv[:, 0:NB - 1, 0:MIX].rearrange("p b c -> p c b"), AX.X, ALU.max))
            c.mark(eng.tensor_tensor(t.k_max[0:LAST, :], t.k_max[0:LAST, :], t.kv[0:LAST, NB - 1, 0:MIX], ALU.max))
            c.then(eng.tensor_reduce(dmax[:, 0:H], t.terms[:, 0:NB - 1, 0:H].rearrange("p b h -> p h b"),
                                     AX.X, ALU.max))
            c.then(eng.tensor_tensor(dmax[0:LAST, 0:H], dmax[0:LAST, 0:H], t.terms[0:LAST, NB - 1, 0:H], ALU.max))
            t.n_dmax = c.n
            eng.wait_ge(dmax_done, 1)
            c.then(eng.tensor_reduce(dmax_col[:, :], ps_t[0:H, 0:P], AX.X, ALU.max))
            c.then(eng.tensor_scalar(dmax_diag[:, :], t.ident[0:H, 0:H], dmax_col[:, 0:1], None, ALU.mult))
            t.n_ddiag = c.n
            eng.wait_ge(dmax_done, 2)
            c.then(eng.tensor_copy(dmax[:, H:2 * H], ps_t[:, P:P + H]))
            c.then(eng.tensor_tensor(u[:, :, :], t.terms[:, :, H:2 * H],
                                     dmax[:, H:2 * H].unsqueeze(1).to_broadcast([P, NB, H]), ALU.add))
            c.mark(eng.scalar_tensor_tensor(t.node[:, :, H:2 * H], u[:, :, :], 0.2, u[:, :, :], ALU.mult, ALU.max))
            c.mark(eng.tensor_copy(t.node[:, :, 0:H], t.terms[:, :, H:2 * H]))
            c.mark(eng.memset(t.node[:, :, 2 * H:3 * H], 1.0))
            c.settle()

        @block.sync
        def _(eng):
            eng.dma_start(src[:, :], io["src"].rearrange("(p f) -> p f", f=EF)).then_inc(edges_in, 16)
            eng.dma_start(dst[:, :], io["dst"].rearrange("(p f) -> p f", f=EF)).then_inc(edges_in, 16)
            eng.wait_ge(made, 1)
            for c in range(7):
                n = 7 if c < 6 else 6
                eng.dma_start(t.acc[:, 7 * c:7 * c + n, 0:C],
                              io["x"][7 * c * P:(7 * c + n) * P, :].rearrange("(b p) c -> p b c", p=P)
                              ).then_inc(x_in[c], 16)
            eng.dma_start(t.acc[0:LAST, NB - 1, 0:C], io["x"][(NB - 1) * P:N, :]).then_inc(x_in[6], 16)
            eng.dma_start(w_all[:, :, 0:C], io["W"].rearrange("(k p) n -> p k n", p=P)).then_inc(weights_in, 16)
            eng.dma_start(w_kv[:, :, :], io["W_qkv"][:, MIX:3 * MIX].rearrange("(k p) n -> p k n", p=P)
                          ).then_inc(weights_in, 16)
            eng.wait_ge(made, 2)
            for h in range(H):
                at = slice((h % 2) * HD, (h % 2) * HD + HD)
                for part, col in ((HD, h), (0, H + h)):
                    eng.dma_start(attn[at, h // 2, col:col + 1],
                                  io["attn_fc"][h:h + 1, part:part + HD].rearrange("o d -> d o")
                                  ).then_inc(weights_in, 16)
            eng.wait_ge(made, 4)
            eng.dma_start(t.table[N:N + 1, :], filler[:, :]).then_inc(filler_in, 16)

            def store(b, par):
                eng.wait_ge(t_out, b + 1)
                eng.dma_start(t.xn_t[bass.ds(b, 1), :, :].rearrange("o p c -> p (o c)"),
                              normed_t[par][:, :, :].rearrange("p k c -> p (k c)")).then_inc(t_stored[par], 16)
                eng.wait_ge(proj_out, 3 * b + 1)
                n = LAST if isinstance(b, int) and b == NB - 1 else P
                eng.dma_start(t.table[bass.ds(b * P, n), :], rows[par][0:n, :]).then_inc(rows_stored[par], 16)

            blocks(nc, eng, 0, NB, store)
            eng.wait_ge(filler_in, 16)
            for par, n in ((0, (NB + 1) // 2), (1, NB // 2)):
                eng.wait_ge(t_stored[par], 16 * n)
                eng.wait_ge(rows_stored[par], 16 * n)

        @block.gpsimd
        def _(eng):
            c = Count(eng, made)
            c.mark(eng.memset(t.acc[:, NB - 1, :], 0.0))
            c.mark(eng.memset(attn[:, :, :], 0.0))
            c.mark(eng.memset(filler[:, 0:C], 0.0))
            c.mark(eng.memset(filler[:, C:TW], -1e30))
            c.mark(eng.memset(kf[0], filler_key()))
            c.mark(eng.iota(lane_i[:, :], [[1, P]], base=0, channel_multiplier=0))
            c.mark(eng.iota(lane_p[:, 0:1], [[0, 1]], base=0, channel_multiplier=1))
            c.mark(eng.iota(t.lane[:, :], [[1, P]], base=0, channel_multiplier=0,
                            allow_small_or_imprecise_dtypes=True))
            c.mark(eng.iota(t.row0[:, :], [[P, NB]], base=0, channel_multiplier=0,
                            allow_small_or_imprecise_dtypes=True))
            c.mark(eng.iota(group_pos[:, :], [[GROUP, NG + 1]], base=0, channel_multiplier=0,
                            allow_small_or_imprecise_dtypes=True))
            c.mark(eng.memset(t.ones[:, :], 1.0))
            c.then(eng.memset(t.ident[:, :], 0.0))
            c.mark(eng.affine_select(out=t.ident[:, :], in_=t.ident[:, :], compare_op=ALU.not_equal,
                                     fill=1.0, base=0, pattern=[[-1, P]], channel_multiplier=1))
            c.mark(eng.tensor_scalar(below[:, :], t.row0[:, 1:NB], -0.5, None, ALU.add))
            c.mark(eng.memset(sign_sum[:, :], 0.0))
            eng.wait_ge(normed_done, NB)
            c.then(eng.memset(t.acc[:, :, :], 0.0))

        @block.scalar
        def _(eng):
            eng.wait_ge(weights_in, 16 * 10)
            eng.wait_ge(w_t_done, 1)
            eng.activation(w_t[:, :, :].rearrange("p k c -> p (k c)"), ps_m[:, :], ACT.Copy).then_inc(w_t_out, 1)
            eng.wait_ge(attn_done, 1)
            eng.activation(w_all[:, :, C:TW + H], ps_kv[:, 0:4 * H].rearrange("p (k n) -> p k n", k=2),
                           ACT.Copy).then_inc(attn_out, 1)
            eng.wait_ge(dve, t.n_moments)
            eng.activation(std[:, :], var[:, :], ACT.Sqrt).then_inc(rooted, 1)

            def project(b, par):
                if not first_or(b, 2):
                    eng.wait_ge(t_done, b - 1)
                eng.activation(normed[par][:, :], t.acc[:, bass.ds(b, 1), 0:C].rearrange("p o c -> p (o c)"),
                               ACT.Identity, bias=shift[:, bass.ds(b, 1)], scale=rstd[:, bass.ds(b, 1)]
                               ).then_inc(normed_done, 1)
                eng.wait_ge(t_done, b + 1)
                if not first_or(b, 2):
                    eng.wait_ge(t_stored[par], (b - par) * 8)
                eng.activation(normed_t[par][:, :, :].rearrange("p k c -> p (k c)"), ps_t[:, 0:C], ACT.Copy
                               ).then_inc(t_out, 1)
                eng.wait_ge(proj_done, b + 1)
                if not first_or(b, 2):
                    eng.wait_ge(rows_stored[par], (b - par) * 8)
                eng.activation(rows[par][:, :], ps_wh[:, 0:TW], ACT.Copy).then_inc(proj_out, 1)
                eng.activation(t.terms[:, bass.ds(b, 1), :].rearrange("p o c -> p (o c)"), ps_wh[:, C:TW + H],
                               ACT.Copy).then_inc(proj_out, 1)
                eng.activation(t.kv[:, bass.ds(b, 1), :].rearrange("p o c -> p (o c)"), ps_kv[:, 0:2 * MIX],
                               ACT.Copy).then_inc(proj_out, 1)

            eng.wait_ge(dve, t.n_norms)
            blocks(nc, eng, 0, NB, project)
            eng.wait_ge(edges_in, 32)
            eng.wait_ge(made, 15)
            eng.activation(sign_out[:, 0:1], src[:, 0:1], ACT.Copy).then_inc(signs, 1)
            with nc.Fori(0, NB - 1, engines=[eng.engine]) as i:
                eng.wait_ge(signs, i + 1)
                eng.activation(sign_out[:, :], src[:, :], ACT.Sign, bias=below[0:EP, bass.ds(i, 1)], scale=-1.0,
                               accum_out=sign_sum[0:EP, bass.ds(i, 1)]).then_inc(signs, 1)

        @block.tensor
        def _(eng):
            eng.wait_ge(made, 13)
            eng.wait_ge(weights_in, 16 * 10)
            for kk in range(2):
                for k in range(2):
                    last = eng.transpose(ps_m[:, kk * C + k * P:kk * C + k * P + P],
                                         w_all[:, k, kk * P:(kk + 1) * P], t.ident[:, :])
            last.then_inc(w_t_done, 1)
            eng.wait_ge(w_t_out, 1)
            for k in range(2):
                for kk in range(2):
                    last = eng.matmul(ps_kv[:, k * 2 * H:(k + 1) * 2 * H], w_t[:, kk, k * P:(k + 1) * P],
                                      attn[:, kk, :], start=(kk == 0), stop=(kk == 1))
            last.then_inc(attn_done, 1)
            eng.wait_ge(attn_out, 1)

            def project(b, par):
                eng.wait_ge(normed_done, b + 1)
                if not first_or(b, 1):
                    eng.wait_ge(t_out, b)
                for k in range(2):
                    last = eng.transpose(ps_t[:, k * P:(k + 1) * P], normed[par][:, k * P:(k + 1) * P],
                                         t.ident[:, :])
                last.then_inc(t_done, 1)
                eng.wait_ge(t_out, b + 1)
                if not first_or(b, 1):
                    eng.wait_ge(proj_out, 3 * b)
                for k in range(2):
                    eng.matmul(ps_wh[:, 0:TW + H], normed_t[par][:, k, :], w_all[:, k, :],
                               start=(k == 0), stop=(k == 1))
                for k in range(2):
                    last = eng.matmul(ps_kv[:, 0:2 * MIX], normed_t[par][:, k, :], w_kv[:, k, :],
                                      start=(k == 0), stop=(k == 1))
                last.then_inc(proj_done, 1)

            def exchange(n):
                eng.wait_ge(dve, t.swap_after[n])
                for s in range(16):
                    last = eng.transpose(swap[s // 4][:, (s % 4) * P:(s % 4 + 1) * P],
                                         kf[t.swap_from[n]][:, s * P:(s + 1) * P], t.ident[:, :])
                    if s % 4 == 3:
                        last.then_inc(swapped, 1)

            blocks(nc, eng, 0, PRE_FIRST, project)
            done = PRE_FIRST
            for m in range(1, 8):
                exchange(2 * m - 2)
                exchange(2 * m - 1)
                if done < NB:
                    blocks(nc, eng, done, min(NB, done + PRE_GAP), project)
                    done = min(NB, done + PRE_GAP)
            exchange(14)
            eng.wait_ge(signs, NB)
            eng.matmul(ps_m[0:NB - 1, 0:1], sign_sum[:, :], t.ones[:, 0:1], start=True, stop=True
                       ).then_inc(counts_done, 1)
            eng.wait_ge(dve, t.n_cmp)
            eng.matmul(ps_wh[:, 0:NG + 1], t.ones[0:NB - 1, :], group_pos[:, :], start=True, stop=True
                       ).then_inc(counts_done, 1)
            eng.wait_ge(dve, t.n_dmax)
            eng.transpose(ps_t[0:H, 0:P], dmax[:, 0:H], t.ident[:, :]).then_inc(dmax_done, 1)
            eng.wait_ge(dve, t.n_ddiag)
            eng.matmul(ps_t[:, P:P + H], t.ones[0:H, :], dmax_diag[:, :], start=True, stop=True
                       ).then_inc(dmax_done, 1)


def gather_and_sum(nc, io, t):
    ctx = ExitStack()
    with ctx:
        sb = lambda name, shape, dt=F32: ctx.enter_context(nc.sbuf_tensor(name, shape, dt))
        pb = lambda name, shape: ctx.enter_context(nc.psum_tensor(name, shape, F32))
        sem = lambda name: ctx.enter_context(nc.semaphore(name))

        k_col = sb("k_col", [P, 1])
        k_diag = sb("k_diag", [P, P])
        k_shift = sb("k_shift", [P, P])
        z_inv = sb("z_inv", [P, 1])
        ctx_t = sb("ctx_t", [P, P])
        ctx_out = sb("ctx_out", [P, C])
        w_q = sb("w_q", [P, 2, MIX])
        w_qt = sb("w_qt", [P, C])
        w_out = sb("w_out", [P, C])
        zeros = sb("zeros", [1, TW])

        index = [sb("index0", [P, TILES], I32), sb("index1", [P, TILES], I32)]
        target = [sb("target0", [P, TILES, TW]), sb("target1", [P, TILES, TW])]
        hot = [sb("hot0", [P, TILES, P]), sb("hot1", [P, TILES, P])]
        hot_t = sb("hot_t", [P, TILES, P])
        off_block = sb("off_block", [P, TILES, H])
        score = sb("score", [P, TILES, H])
        leaky = sb("leaky", [P, TILES, H])
        exponent = sb("exponent", [P, TILES, H])
        weighed = sb("weighed", [P, TILES, TW])

        ps_hot = [pb("ps_hot0", [P, 512]), pb("ps_hot1", [P, 512])]
        ps_node = pb("ps_node", [P, TILES, 3 * H])
        ps_sum = pb("ps_sum", [P, 512])
        ps_a = pb("ps_a", [P, 512])
        ps_b = pb("ps_b", [P, 512])
        ps_ctx = pb("ps_ctx", [P, P])
        ps_z = pb("ps_z", [P, 2])

        mix_in = sem("mix_in")
        pre_v = sem("pre_v")
        pre_t = sem("pre_t")
        k_exp = sem("k_exp")
        index_ready = sem("index_ready")
        gathered = [sem("gathered0"), sem("gathered1")]
        used = [sem("used0"), sem("used1")]
        hot_ready = sem("hot_ready")
        hot_turned = sem("hot_turned")
        hot_t_ready = sem("hot_t_ready")
        node_ready = sem("node_ready")
        steps = sem("steps")
        score_ready = sem("score_ready")
        exp_ready = sem("exp_ready")
        weighed_ready = sem("weighed_ready")
        summed = sem("summed")
        added = sem("added")

        block = ctx.enter_context(nc.Block())

        def visits(eng, body, before=None, after=None):
            with nc.Fori(0, NG // 2, engines=[eng.engine]) as i:
                for par in range(2):
                    g = 2 * i + par
                    lo = eng.value_load(t.first_block[0:1, bass.ds(g, 1)], min_val=0, max_val=NB - 1)
                    hi = eng.value_load(t.first_block[0:1, bass.ds(g + 1, 1)], min_val=0, max_val=NB - 1)
                    if before:
                        before(i, par)
                        eng.nop(nofuse=True)
                    with nc.Fori(lo, hi + 1, engines=[eng.engine]) as bb:
                        b = bb.with_bounds(min_val=0, max_val=NB - 1)
                        body(g, b, g + b, par, lo)
                    if after:
                        after(g + hi + 1, par)

        def later(b, lo):
            return ((b - lo + 63) >> 6) & 1

        @block.sync
        def _(eng):
            eng.dma_start(w_q[:, :, :], io["W_qkv"][:, 0:MIX].rearrange("(k p) n -> p k n", p=P)).then_inc(mix_in, 16)
            eng.dma_start(w_out[:, :], io["W_out"]).then_inc(mix_in, 16)

        @block.gpsimd
        def _(eng):
            with nc.Fori(0, NG // 2, engines=[eng.engine]) as i:
                for par in range(2):
                    g = 2 * i + par
                    eng.wait_ge(used[par], i + 1)
                    eng.tensor_copy(index[par][:, :], t.edge_col[:, bass.ds(TILES * g, TILES)]
                                    ).then_inc(index_ready, 1)
                    eng.wait_ge(index_ready, g + 1)
                    eng.nop(nofuse=True)
                    for k in range(TILES):
                        eng.indirect_dma_start(target[par][:, k, :], None, t.table[:, :],
                                               bass.IndirectOffsetOnAxis(ap=index[par][:, k:k + 1], axis=0)
                                               ).then_inc(gathered[par], 16)

        @block.scalar
        def _(eng):
            eng.wait_ge(pre_v, 4)
            eng.activation(t.kv[:, :, 0:MIX], t.kv[:, :, 0:MIX], ACT.Exp).then_inc(k_exp, 1)

            def visit(g, b, v, par, lo):
                eng.wait_ge(hot_turned, v + 1)
                eng.activation(hot_t[:, :, :].rearrange("p t e -> p (t e)"), ps_hot[par][:, :], ACT.Copy
                               ).then_inc(hot_t_ready, 1)
                eng.wait_ge(score_ready, v + 1)
                eng.activation(weighed[:, :, C:TW], exponent[:, :, :], ACT.Exp).then_inc(exp_ready, 1)

            visits(eng, visit)

        @block.tensor
        def _(eng):
            eng.transpose(ps_a[:, 0:P], t.k_max[:, :], t.ident[:, :]).then_inc(pre_t, 1)
            eng.wait_ge(mix_in, 32)
            for k in range(2):
                last = eng.transpose(ps_b[:, k * P:(k + 1) * P], w_q[:, k, :], t.ident[:, :])
            last.then_inc(pre_t, 1)
            eng.wait_ge(pre_v, 2)
            eng.matmul(ps_a[:, P:2 * P], t.ones[:, :], k_diag[:, :], start=True, stop=True).then_inc(pre_t, 1)
            eng.wait_ge(pre_v, 5)
            for _ in range(2):
                eng.matmul(ps_sum[:, 0:TW], zeros[0:1, 0:P], zeros[0:1, :], start=True, stop=True
                           ).then_inc(summed, 1)
            eng.wait_ge(k_exp, 1)
            for b in range(NB):
                n = P if b < NB - 1 else LAST
                eng.matmul(ps_ctx[:, :], t.kv[0:n, b, MIX:2 * MIX], t.kv[0:n, b, 0:MIX],
                           start=(b == 0), stop=(b == NB - 1))
                last = eng.matmul(ps_z[:, 0:1], t.kv[0:n, b, 0:MIX], t.ones[0:n, 0:1],
                                  start=(b == 0), stop=(b == NB - 1))
            last.then_inc(pre_t, 1)
            eng.wait_ge(pre_v, 11)
            eng.matmul(ps_a[:, 0:C], ctx_t[:, :], w_out[:, :], start=True, stop=True).then_inc(pre_t, 1)
            eng.wait_ge(pre_v, 14)
            for k in range(2):
                last = eng.matmul(ps_b[:, k * C:(k + 1) * C], w_qt[:, k * P:(k + 1) * P], ctx_out[:, :],
                                  start=True, stop=True)
            last.then_inc(pre_t, 1)

            def visit(g, b, v, par, lo):
                eng.wait_ge(hot_ready, v + 1)
                for k in range(TILES):
                    last = eng.transpose(ps_hot[par][:, k * P:(k + 1) * P], hot[par][:, k, :], t.ident[:, :])
                last.then_inc(hot_turned, 1)
                eng.wait_ge(hot_t_ready, v + 1)
                for k in range(TILES):
                    last = eng.matmul(ps_node[:, k, :], hot_t[:, k, :],
                                      t.node[:, bass.ds(b, 1), :].rearrange("p o c -> p (o c)"),
                                      start=True, stop=True)
                last.then_inc(node_ready, 1)
                eng.wait_ge(weighed_ready, v + 1)
                for k in range(TILES):
                    last = eng.matmul(ps_sum[:, 0:TW], hot[par][:, k, :], weighed[:, k, :],
                                      start=(k == 0), stop=(k == TILES - 1))
                last.then_inc(summed, 1)

            visits(eng, visit)

        @block.vector
        def _(eng):
            for ready in (*used, added):
                eng.sem_inc(ready, 1)
            c = Count(eng, pre_v)
            eng.wait_ge(pre_t, 1)
            c.then(eng.tensor_reduce(k_col[:, :], ps_a[:, 0:P], AX.X, ALU.max))
            c.mark(eng.tensor_scalar(k_diag[:, :], t.ident[:, :], k_col[:, 0:1], None, ALU.mult))
            eng.wait_ge(pre_t, 3)
            c.then(eng.tensor_copy(k_shift[:, :], ps_a[:, P:2 * P]))
            c.mark(eng.tensor_tensor(t.kv[:, :, 0:MIX], t.kv[:, :, 0:MIX],
                                     k_shift[:, :].unsqueeze(1).to_broadcast([P, NB, MIX]), ALU.subtract))
            c.mark(eng.memset(zeros[:, :], 0.0))
            c.mark(eng.memset(t.score_max[:, :, :], -1e30))
            c.then(eng.memset(ctx_t[:, :], 0.0))
            eng.wait_ge(pre_t, 4)
            for h in range(MH):
                s = slice(h * MD, (h + 1) * MD)
                c.mark(eng.tensor_copy(ctx_t[s, s], ps_ctx[s, s]))
            c.mark(eng.tensor_copy(w_qt[:, :], ps_b[:, 0:C]))
            c.then(eng.reciprocal(z_inv[:, :], ps_z[:, 0:1]))
            eng.wait_ge(pre_t, 5)
            c.mark(eng.tensor_scalar(ctx_out[:, :], ps_a[:, 0:C], z_inv[:, 0:1], MD ** -0.5,
                                     ALU.mult, ALU.mult))
            eng.wait_ge(pre_t, 6)
            c.mark(eng.tensor_copy(t.mixer[:, :, :].rearrange("p k n -> p (k n)"), ps_b[:, :]))

            def add_last(b, v):
                eng.wait_ge(summed, v + 2)
                eng.wait_ge(added, v + 1)
                rows = t.acc[:, bass.ds(b, 1), :].rearrange("p o c -> p (o c)")
                eng.tensor_tensor(rows, rows, ps_sum[:, 0:TW], ALU.add).then_inc(added, 1)

            def arrived(i, par):
                eng.wait_ge(gathered[par], 16 * TILES * (i + 1))

            def visit(g, b, v, par, lo):
                eng.wait_ge(summed, v + 1 + later(b, lo))
                eng.scalar_tensor_tensor(
                    hot[par][:, :, :], t.edge_row[:, bass.ds(TILES * g, TILES)].unsqueeze(2).to_broadcast([P, TILES, P]),
                    t.row0[:, bass.ds(b, 1)], t.lane[:, :].unsqueeze(1).to_broadcast([P, TILES, P]),
                    ALU.subtract, ALU.is_equal).then_inc(hot_ready, 1)
                add_last((b - later(b, lo)).with_bounds(min_val=0, max_val=NB - 1), v)
                eng.wait_ge(node_ready, v + 1)
                eng.tensor_scalar(off_block[:, :, :], ps_node[:, :, 2 * H:3 * H], 1e30, -1e30, ALU.mult, ALU.add
                                  ).then_inc(steps, 1)
                eng.tensor_tensor(score[:, :, :], ps_node[:, :, 0:H], target[par][:, :, C:TW], ALU.add
                                  ).then_inc(steps, 1)
                eng.wait_ge(steps, 5 * v + 2)
                eng.tensor_tensor(score[:, :, :], score[:, :, :], off_block[:, :, :], ALU.add).then_inc(steps, 1)
                eng.wait_ge(steps, 5 * v + 3)
                eng.tensor_tensor(t.score_max[:, :, :], t.score_max[:, :, :], score[:, :, :], ALU.max
                                  ).then_inc(steps, 1)
                eng.scalar_tensor_tensor(leaky[:, :, :], score[:, :, :], 0.2, score[:, :, :], ALU.mult, ALU.max
                                         ).then_inc(steps, 1)
                eng.wait_ge(steps, 5 * v + 5)
                eng.tensor_tensor(exponent[:, :, :], leaky[:, :, :], ps_node[:, :, H:2 * H], ALU.subtract
                                  ).then_inc(score_ready, 1)
                eng.wait_ge(exp_ready, v + 1)
                eng.tensor_tensor(weighed[:, :, 0:C].rearrange("p t (h d) -> p t h d", h=H),
                                  target[par][:, :, 0:C].rearrange("p t (h d) -> p t h d", h=H),
                                  weighed[:, :, C:TW].unsqueeze(3).to_broadcast([P, TILES, H, HD]), ALU.mult
                                  ).then_inc(weighed_ready, 1)

            def finish(n, par):
                eng.wait_ge(weighed_ready, n)
                eng.sem_inc(used[par], 1)

            visits(eng, visit, arrived, finish)
            add_last(NB - 1, NG + NB - 1)
            eng.wait_ge(added, NG + NB + 1)


def mix_nodes(nc, io, t):
    ctx = ExitStack()
    with ctx:
        sb = lambda name, shape, dt=F32: ctx.enter_context(nc.sbuf_tensor(name, shape, dt))
        pb = lambda name, shape: ctx.enter_context(nc.psum_tensor(name, shape, F32))
        sem = lambda name: ctx.enter_context(nc.semaphore(name))

        top = sb("top", [P, H])
        top_col = sb("top_col", [H, 2])
        top_diag = sb("top_diag", [H, H])
        floor = sb("floor", [P, NB, H])
        denom = sb("denom", [P, NB, H])
        w_ffn = sb("w_ffn", [P, 2, C])
        w_gamma = sb("w_gamma", [P, 2, C])
        gamma = sb("gamma", [P, 2])
        beta = sb("beta", [P, 2])
        beta_rows = sb("beta_rows", [P, 2, P])
        ffn_bias = sb("ffn_bias", [P, C])
        mix_bias = sb("mix_bias", [P, C])
        stats = sb("stats_g", [P, NB, 6])
        tmp = sb("tmp_g", [P, 4, NB])
        mean2 = sb("mean2_g", [P, NB])
        var = sb("var_g", [P, NB])
        std = sb("std_g", [P, NB])
        rstd = sb("rstd_g", [P, NB])
        shift = sb("shift_g", [P, NB])
        wh = [sb("wh0", [P, C]), sb("wh1", [P, C])]
        x_in = [sb("x_in0", [P, C]), sb("x_in1", [P, C])]
        xn_t = [sb("xn_t0", [P, 2, P]), sb("xn_t1", [P, 2, P])]
        normed = [sb("normed_g0", [P, C]), sb("normed_g1", [P, C])]
        normed_t = [sb("normed_gt0", [P, 2, P]), sb("normed_gt1", [P, 2, P])]
        gnn = sb("gnn", [P, C])
        mixed = sb("mixed", [P, C])

        ps_t = [pb("ps_gt0", [P, 512]), pb("ps_gt1", [P, 512])]
        ps_both = [pb("ps_both0", [P, 512]), pb("ps_both1", [P, 512])]
        ps_m = pb("ps_gm", [P, 512])

        params_in = sem("params_in")
        wh_in = [sem("wh_in0"), sem("wh_in1")]
        x_loaded = [sem("x_loaded0"), sem("x_loaded1")]
        dve = sem("dve_g")
        pe = sem("pe_g")
        act = sem("act_g")
        wh_added = sem("wh_added")
        wh_stats = sem("wh_stats")
        normed_done = sem("normed_g_done")
        t_done = sem("t_g_done")
        t_out = sem("t_g_out")
        both_done = sem("both_done")
        step = sem("mix_step")

        block = ctx.enter_context(nc.Block())

        @block.vector
        def _(eng):
            c = Count(eng, dve)
            c.mark(eng.tensor_reduce(top[:, :], t.score_max[:, :, :].rearrange("p t h -> p h t"), AX.X, ALU.max))
            eng.wait_ge(pe, 1)
            c.then(eng.tensor_reduce(top_col[:, 0:1], ps_m[0:H, 0:P], AX.X, ALU.max))
            c.then(eng.scalar_tensor_tensor(top_col[:, 1:2], top_col[:, 0:1], 0.2, top_col[:, 0:1],
                                            ALU.mult, ALU.max))
            c.mark(eng.tensor_scalar(top_diag[:, :], t.ident[0:H, 0:H], top_col[:, 1:2], None, ALU.mult))
            t.n_top = c.n
            eng.wait_ge(params_in, 16 * 5)
            for k in range(2):
                c.mark(eng.tensor_scalar(w_gamma[:, k, :], w_ffn[:, k, :], gamma[:, k:k + 1], None, ALU.mult))
                c.mark(eng.tensor_scalar(beta_rows[:, k, :], t.ones[:, :], beta[:, k:k + 1], None, ALU.mult))
            t.n_beta = c.n
            eng.wait_ge(pe, 2)
            c.then(eng.tensor_copy(top[:, :], ps_m[:, P:P + H]))
            c.mark(eng.tensor_tensor(floor[:, :, :], top[:, :].unsqueeze(1).to_broadcast([P, NB, H]),
                                     t.node[:, :, H:2 * H], ALU.subtract))
            t.n_floor = c.n
            eng.wait_ge(act, 1)
            c.then(eng.scalar_tensor_tensor(denom[:, :, :], floor[:, :, :], 1e-15, t.acc[:, :, C:TW],
                                            ALU.mult, ALU.add))
            c.then(eng.tensor_scalar(denom[:, :, :], denom[:, :, :], 1e-37, None, ALU.max))
            c.then(eng.reciprocal(denom[:, :, :], denom[:, :, :]))
            heads = t.acc[:, :, 0:C].rearrange("p b (h d) -> p b h d", h=H)
            c.then(eng.tensor_tensor(heads, heads, denom[:, :, :].unsqueeze(3).to_broadcast([P, NB, H, HD]), ALU.mult))
            eng.wait_ge(pe, 3)
            c.then(eng.tensor_tensor(ffn_bias[:, :], ffn_bias[:, :], ps_m[:, 0:C], ALU.add))

            def add_wh(b, par):
                n = LAST if isinstance(b, int) and b == NB - 1 else P
                eng.wait_ge(wh_in[par], 8 * (b - par) + 16)
                row = t.acc[0:n, bass.ds(b, 1), 0:C].rearrange("p o c -> p (o c)")
                eng.tensor_tensor(row, row, wh[par][0:n, :], ALU.add).then_inc(wh_added, 1)
                eng.wait_ge(wh_added, b + 1)
                eng.bn_stats(stats[:, bass.ds(b, 1), :].rearrange("p o c -> p (o c)"),
                             t.acc[:, bass.ds(b, 1), 0:C].rearrange("p o c -> p (o c)")).then_inc(wh_stats, 1)

            blocks(nc, eng, 0, NB, add_wh)
            eng.wait_ge(wh_stats, NB)
            moments(eng, c, stats, tmp, mean2[:, :], var[:, :])
            t.n_var = c.n
            eng.wait_ge(act, 2)
            c.then(eng.reciprocal(rstd[:, :], std[:, :]))
            c.then(eng.scalar_tensor_tensor(shift[:, :], mean2[:, :], -0.5, rstd[:, :], ALU.mult, ALU.mult))
            t.n_rstd = c.n

            def mix(b, par):
                n = LAST if isinstance(b, int) and b == NB - 1 else P
                c = Count(eng, step)
                c.n = 5 * b
                eng.wait_ge(both_done, b + 1)
                eng.wait_ge(x_loaded[par], 16 * (b - par) + 32)
                c.mark(eng.tensor_tensor(gnn[0:n, :], ps_both[par][0:n, 0:C], ffn_bias[0:n, :], ALU.add))
                c.then(eng.tensor_tensor(mixed[0:n, :], ps_both[par][0:n, C:2 * C], mix_bias[0:n, :], ALU.add))
                c.then(eng.scalar_tensor_tensor(gnn[0:n, :], gnn[0:n, :], 0.0, x_in[par][0:n, :], ALU.max, ALU.add))
                c.then(eng.tensor_tensor(t.acc[0:n, bass.ds(b, 1), 0:C].rearrange("p o c -> p (o c)"),
                                         gnn[0:n, :], mixed[0:n, :], ALU.add))
                c.mark(eng.bn_stats(t.stats[:, bass.ds(b, 1), :].rearrange("p o c -> p (o c)"),
                                    t.acc[:, bass.ds(b, 1), 0:C].rearrange("p o c -> p (o c)")))

            blocks(nc, eng, 0, NB, mix)

        @block.sync
        def _(eng):
            eng.dma_start(w_ffn[:, :, :], io["ffn_w"].rearrange("(k p) n -> p k n", p=P)).then_inc(params_in, 16)
            eng.dma_start(gamma[:, :], io["gamma"].rearrange("(k p) -> p k", p=P), allow_slow_non_contiguous=True).then_inc(params_in, 16)
            eng.dma_start(beta[:, :], io["beta"].rearrange("(k p) -> p k", p=P), allow_slow_non_contiguous=True).then_inc(params_in, 16)
            eng.dma_start(ffn_bias[:, :], io["ffn_b"].partition_broadcast(P)).then_inc(params_in, 16)
            eng.dma_start(mix_bias[:, :], io["b_out"].partition_broadcast(P)).then_inc(params_in, 16)

            def load_wh(b, par):
                n = LAST if isinstance(b, int) and b == NB - 1 else P
                if not first_or(b, 2):
                    eng.wait_ge(wh_added, b - 1)
                eng.dma_start(wh[par][0:n, :], t.table[bass.ds(b * P, n), 0:C]).then_inc(wh_in[par], 16)

            blocks(nc, eng, 0, NB, load_wh)

            def load_x(b, par):
                n = LAST if isinstance(b, int) and b == NB - 1 else P
                if not first_or(b, 2):
                    eng.wait_ge(step, 5 * b - 5)
                eng.dma_start(x_in[par][0:n, :], io["x"][bass.ds(b * P, n), :]).then_inc(x_loaded[par], 16)
                eng.dma_start(xn_t[par][:, :, :].rearrange("p k c -> p (k c)"),
                              t.xn_t[bass.ds(b, 1), :, :].rearrange("o p c -> p (o c)")).then_inc(x_loaded[par], 16)

            blocks(nc, eng, 0, NB, load_x)

        @block.scalar
        def _(eng):
            eng.wait_ge(dve, t.n_floor)
            eng.activation(floor[:, :, :], floor[:, :, :], ACT.Exp).then_inc(act, 1)
            eng.wait_ge(dve, t.n_var)
            eng.activation(std[:, :], var[:, :], ACT.Sqrt).then_inc(act, 1)
            eng.wait_ge(dve, t.n_rstd)

            def normalise(b, par):
                if not first_or(b, 2):
                    eng.wait_ge(t_done, b - 1)
                eng.activation(normed[par][:, :], t.acc[:, bass.ds(b, 1), 0:C].rearrange("p o c -> p (o c)"),
                               ACT.Identity, bias=shift[:, bass.ds(b, 1)], scale=rstd[:, bass.ds(b, 1)]
                               ).then_inc(normed_done, 1)

            def turned(b, par):
                eng.wait_ge(t_done, b + 1)
                if not first_or(b, 2):
                    eng.wait_ge(both_done, b - 1)
                eng.activation(normed_t[par][:, :, :].rearrange("p k c -> p (k c)"), ps_t[par][:, 0:C], ACT.Copy
                               ).then_inc(t_out, 1)

            normalise(0, 0)

            def both(b, par):
                normalise(b + 1, 1 - par)
                turned(b, par)

            blocks(nc, eng, 0, NB - 1, both)
            turned(NB - 1, (NB - 1) % 2)

        @block.tensor
        def _(eng):
            eng.wait_ge(dve, 1)
            eng.transpose(ps_m[0:H, 0:P], top[:, :], t.ident[:, :]).then_inc(pe, 1)
            eng.wait_ge(dve, t.n_top)
            eng.matmul(ps_m[:, P:P + H], t.ones[0:H, :], top_diag[:, :], start=True, stop=True).then_inc(pe, 1)
            eng.wait_ge(dve, t.n_floor)
            for k in range(2):
                last = eng.matmul(ps_m[:, 0:C], beta_rows[:, k, :], w_ffn[:, k, :], start=(k == 0), stop=(k == 1))
            last.then_inc(pe, 1)

            def turn(b, par):
                eng.wait_ge(normed_done, b + 1)
                if not first_or(b, 2):
                    eng.wait_ge(t_out, b - 1)
                for k in range(2):
                    last = eng.transpose(ps_t[par][:, k * P:(k + 1) * P], normed[par][:, k * P:(k + 1) * P],
                                         t.ident[:, :])
                last.then_inc(t_done, 1)

            def multiply(b, par):
                eng.wait_ge(t_out, b + 1)
                eng.wait_ge(x_loaded[par], 16 * (b - par) + 32)
                if not first_or(b, 2):
                    eng.wait_ge(step, 5 * b - 5)
                for k in range(2):
                    eng.matmul(ps_both[par][:, 0:C], normed_t[par][:, k, :], w_gamma[:, k, :],
                               start=(k == 0), stop=(k == 1))
                for k in range(2):
                    last = eng.matmul(ps_both[par][:, C:2 * C], xn_t[par][:, k, :], t.mixer[:, k, :],
                                      start=(k == 0), stop=(k == 1))
                last.then_inc(both_done, 1)

            turn(0, 0)

            def both(b, par):
                turn(b + 1, 1 - par)
                multiply(b, par)

            blocks(nc, eng, 0, NB - 1, both)
            multiply(NB - 1, (NB - 1) % 2)


def experts(nc, io, t):
    ctx = ExitStack()
    with ctx:
        sb = lambda name, shape, dt=F32: ctx.enter_context(nc.sbuf_tensor(name, shape, dt))
        pb = lambda name, shape: ctx.enter_context(nc.psum_tensor(name, shape, F32))
        sem = lambda name: ctx.enter_context(nc.semaphore(name))
        KC = HID // P
        SM = 9

        w1 = sb("w1", [P, 2, HID])
        b1 = sb("b1", [P, KC])
        wg = sb("wg", [P, KC, NE])
        bg = sb("bg", [P, NE])
        wd = sb("wd", [P, KC, NE * C])
        bd = sb("bd", [P, NE * C])
        rank = sb("rank", [P, NE])
        tmp = sb("tmp_e", [P, 4, NB])
        mean2 = sb("mean2_e", [P, NB])
        var = sb("var_e", [P, NB])
        std = sb("std_e", [P, NB])
        rstd = sb("rstd_e", [P, NB])
        shift = sb("shift_e", [P, NB])
        normed = [sb("normed_e0", [P, C]), sb("normed_e1", [P, C])]
        normed_t = [sb("normed_et0", [P, 2, P]), sb("normed_et1", [P, 2, P])]
        hidden = [sb("hidden0", [P, KC, P]), sb("hidden1", [P, KC, P])]
        logits = sb("logits", [P, NE])
        one = sb("one", [P, 4])
        probs = sb("probs", [P, NE])
        hits = sb("hits", [P, NE])
        share = sb("share", [P, NE])
        result = [sb("result0", [P, C]), sb("result1", [P, C])]

        ps_t = pb("ps_et", [P, 512])
        ps_h = [pb("ps_h0", [P, 512]), pb("ps_h1", [P, 512])]
        ps_gate = pb("ps_gate", [P, 512])
        ps_y = [pb(f"ps_y{q}", [P, 512]) for q in range(4)]

        params_in = sem("expert_params_in")
        weights_in = sem("expert_weights_in")
        ranked = sem("ranked")
        dve = sem("dve_e")
        rooted = sem("rooted_e")
        normed_done = sem("normed_e_done")
        t_done = sem("t_e_done")
        t_out = sem("t_e_out")
        h_done = sem("h_done")
        h_out = sem("h_out")
        gate_done = sem("gate_done")
        gate = sem("gate")
        exp_done = sem("exp_done")
        y_done = sem("y_done")
        combined = sem("combined")
        stored = [sem("stored0"), sem("stored1")]

        block = ctx.enter_context(nc.Block())

        @block.vector
        def _(eng):
            c = Count(eng, dve)
            moments(eng, c, t.stats, tmp, mean2[:, :], var[:, :])
            t.n_var = c.n
            eng.wait_ge(rooted, 1)
            c.then(eng.reciprocal(rstd[:, :], std[:, :]))
            c.then(eng.scalar_tensor_tensor(shift[:, :], mean2[:, :], -0.5, rstd[:, :], ALU.mult, ALU.mult))
            t.n_rstd = c.n
            eng.wait_ge(params_in, 16 * 5)
            eng.wait_ge(ranked, 1)

            def choose(b, par):
                g = Count(eng, gate)
                g.n = SM * b
                eng.wait_ge(gate_done, b + 1)
                g.then(eng.tensor_tensor(logits[:, :], ps_gate[:, 0:NE], bg[:, :], ALU.add))
                g.then(eng.tensor_reduce(one[:, 0:1], logits[:, :], AX.X, ALU.max))
                g.mark(eng.tensor_scalar(logits[:, :], logits[:, :], one[:, 0:1], None, ALU.subtract))
                eng.wait_ge(exp_done, b + 1)
                g.then(eng.reciprocal(one[:, 2:3], one[:, 1:2]))
                g.then(eng.tensor_scalar(probs[:, :], probs[:, :], one[:, 2:3], None, ALU.mult))
                g.then(eng.tensor_reduce(one[:, 3:4], probs[:, :], AX.X, ALU.max))
                g.then(eng.scalar_tensor_tensor(hits[:, :], probs[:, :], one[:, 3:4], rank[:, :],
                                                ALU.is_equal, ALU.mult))
                g.then(eng.tensor_reduce(one[:, 0:1], hits[:, :], AX.X, ALU.max))
                g.then(eng.scalar_tensor_tensor(share[:, :], rank[:, :], one[:, 0:1], probs[:, :],
                                                ALU.is_equal, ALU.mult))
                if not first_or(b, 2):
                    eng.wait_ge(stored[par], 8 * (b - par))
                k = Count(eng, combined)
                k.n = 2 * NE * b
                out = result[par][:, :]
                last = t.acc[:, bass.ds(b, 1), 0:C].rearrange("p o c -> p (o c)")
                for e in range(NE):
                    k.then(eng.scalar_tensor_tensor(out, bd[:, e * C:(e + 1) * C], share[:, e:e + 1], last,
                                                    ALU.mult, ALU.add))
                    last = out
                for e in range(NE):
                    if e % 2 == 0:
                        eng.wait_ge(y_done, 4 * b + e // 2 + 1)
                    k.then(eng.scalar_tensor_tensor(out, ps_y[e // 2][:, (e % 2) * C:(e % 2 + 1) * C],
                                                    share[:, e:e + 1], out, ALU.mult, ALU.add))

            blocks(nc, eng, 0, NB, choose)

        @block.gpsimd
        def _(eng):
            eng.iota(rank[:, :], [[-1, NE]], base=NE, channel_multiplier=0,
                     allow_small_or_imprecise_dtypes=True).then_inc(ranked, 1)

        @block.sync
        def _(eng):
            eng.dma_start(w1[:, :, :], io["W1"].rearrange("(k p) n -> p k n", p=P)).then_inc(params_in, 16)
            eng.dma_start(b1[:, :], io["b1"].rearrange("(k p) -> p k", p=P), allow_slow_non_contiguous=True
                          ).then_inc(params_in, 16)
            eng.dma_start(wg[:, :, :], io["Wg"].rearrange("(k p) n -> p k n", p=P)).then_inc(params_in, 16)
            eng.dma_start(bg[:, :], io["bg"].partition_broadcast(P)).then_inc(params_in, 16)
            eng.dma_start(bd[:, :], io["bd"].rearrange("e n -> (e n)").partition_broadcast(P)).then_inc(params_in, 16)
            for e in range(NE):
                eng.dma_start(wd[:, :, e * C:(e + 1) * C], io["Wd"][e, :, :].rearrange("(k p) n -> p k n", p=P)
                              ).then_inc(weights_in, 16)

            def store(b, par):
                n = LAST if isinstance(b, int) and b == NB - 1 else P
                eng.wait_ge(combined, 2 * NE * (b + 1))
                eng.dma_start(io["out"][bass.ds(b * P, n), :], result[par][0:n, :]).then_inc(stored[par], 16)

            blocks(nc, eng, 0, NB, store)
            eng.wait_ge(stored[0], 16 * ((NB + 1) // 2))
            eng.wait_ge(stored[1], 16 * (NB // 2))

        @block.scalar
        def _(eng):
            eng.wait_ge(dve, t.n_var)
            eng.activation(std[:, :], var[:, :], ACT.Sqrt).then_inc(rooted, 1)
            eng.wait_ge(dve, t.n_rstd)
            eng.wait_ge(params_in, 16 * 5)

            def front(b, par):
                if not first_or(b, 2):
                    eng.wait_ge(t_done, b - 1)
                eng.activation(normed[par][:, :], t.acc[:, bass.ds(b, 1), 0:C].rearrange("p o c -> p (o c)"),
                               ACT.Identity, bias=shift[:, bass.ds(b, 1)], scale=rstd[:, bass.ds(b, 1)]
                               ).then_inc(normed_done, 1)
                eng.wait_ge(t_done, b + 1)
                if not first_or(b, 2):
                    eng.wait_ge(h_done, 2 * (b - 1))
                eng.activation(normed_t[par][:, :, :].rearrange("p k c -> p (k c)"), ps_t[:, 0:C], ACT.Copy
                               ).then_inc(t_out, 1)
                if not first_or(b, 2):
                    eng.wait_ge(y_done, 4 * (b - 1))
                for j in range(KC):
                    if j % 4 == 0:
                        eng.wait_ge(h_done, 2 * b + j // 4 + 1)
                    eng.activation(hidden[par][:, j, :], ps_h[j // 4][:, (j % 4) * P:(j % 4 + 1) * P], ACT.Gelu,
                                   bias=b1[:, j:j + 1]).then_inc(h_out, 1)

            def back(b):
                eng.wait_ge(gate, SM * b + 3)
                eng.activation(probs[:, :], logits[:, :], ACT.Exp, accum_out=one[:, 1:2]).then_inc(exp_done, 1)

            front(0, 0)

            def both(b, par):
                front(b + 1, 1 - par)
                back(b)

            blocks(nc, eng, 0, NB - 1, both)
            back(NB - 1)

        @block.tensor
        def _(eng):
            eng.wait_ge(params_in, 16 * 5)

            def front(b, par):
                eng.wait_ge(normed_done, b + 1)
                if not first_or(b, 1):
                    eng.wait_ge(t_out, b)
                for k in range(2):
                    last = eng.transpose(ps_t[:, k * P:(k + 1) * P], normed[par][:, k * P:(k + 1) * P],
                                         t.ident[:, :])
                last.then_inc(t_done, 1)
                eng.wait_ge(t_out, b + 1)
                if not first_or(b, 1):
                    eng.wait_ge(h_out, KC * b)
                for j in range(KC):
                    for k in range(2):
                        last = eng.matmul(ps_h[j // 4][:, (j % 4) * P:(j % 4 + 1) * P],
                                          w1[:, k, j * P:(j + 1) * P], normed_t[par][:, k, :],
                                          start=(k == 0), stop=(k == 1))
                    if j % 4 == 3:
                        last.then_inc(h_done, 1)

            def back(b, par):
                eng.wait_ge(h_out, KC * b + KC)
                if not first_or(b, 1):
                    eng.wait_ge(gate, SM * b)
                for j in range(KC):
                    last = eng.matmul(ps_gate[:, 0:NE], hidden[par][:, j, :], wg[:, j, :],
                                      start=(j == 0), stop=(j == KC - 1))
                last.then_inc(gate_done, 1)
                for q in range(4):
                    if not first_or(b, 1):
                        eng.wait_ge(combined, 2 * NE * b - NE + 2 * q + 2)
                    for j in range(KC):
                        last = eng.matmul(ps_y[q][:, :], hidden[par][:, j, :], wd[:, j, 512 * q:512 * (q + 1)],
                                          start=(j == 0), stop=(j == KC - 1))
                    last.then_inc(y_done, 1)

            front(0, 0)
            eng.wait_ge(weights_in, 16 * NE)

            def both(b, par):
                front(b + 1, 1 - par)
                back(b, par)

            blocks(nc, eng, 0, NB - 1, both)
            back(NB - 1, (NB - 1) % 2)


def graph_layers(nc, io):
    ctx = ExitStack()
    with ctx:
        sb = lambda name, shape, dt=F32: ctx.enter_context(nc.sbuf_tensor(name, shape, dt))
        t = Tiles()
        t.table = nc.dram_tensor("table", [N + 1, TW], F32, kind="Internal").ap()
        t.xn_t = nc.dram_tensor("xn_t", [NB, P, C], F32, kind="Internal").ap()
        t.acc = sb("acc", [P, NB, TW])
        t.node = sb("node", [P, NB, 3 * H])
        t.lane = sb("lane", [P, P])
        t.row0 = sb("row0", [P, NB])
        t.ones = sb("ones", [P, P])
        t.ident = sb("ident", [P, P])
        t.mixer = sb("mixer", [P, 2, C])
        t.score_max = sb("score_max", [P, TILES, H])
        t.stats = sb("stats_x", [P, NB, 6])
        with ExitStack() as graph:
            sb = lambda name, shape, dt=F32: graph.enter_context(nc.sbuf_tensor(name, shape, dt))
            t.kv = sb("kv", [P, NB, 2 * MIX])
            t.k_max = sb("k_max", [P, P])
            t.terms = sb("terms", [P, NB, 2 * H])
            t.edge_col = sb("edge_col", [P, FREE], I32)
            t.edge_row = sb("edge_row", [P, FREE])
            t.first_block = sb("first_block", [1, NG + 1], I32)
            sort_and_project(nc, io, t)
            gather_and_sum(nc, io, t)
        mix_nodes(nc, io, t)
        experts(nc, io, t)


_INS = {"x": "x", "src": "src", "dst": "dst", "W": "L0_gnn_W", "attn_fc": "L0_gnn_attn_fc",
        "gamma": "L0_gnn_ln_gamma", "beta": "L0_gnn_ln_beta", "ffn_w": "L0_gnn_ffn_w", "ffn_b": "L0_gnn_ffn_b",
        "W_qkv": "L0_mix_W_qkv", "W_out": "L0_mix_W_out", "b_out": "L0_mix_b_out", "W1": "L0_ffn_W1",
        "b1": "L0_ffn_b1", "Wg": "L0_ffn_Wg", "bg": "L0_ffn_bg", "Wd": "L0_ffn_Wd", "bd": "L0_ffn_bd"}


def kernel(**inputs):
    import concourse.bacc as bacc
    from concourse.bass_utils import run_bass_kernel_spmd

    nc = bacc.Bacc("TRN2", target_bir_lowering=False, num_devices=1)
    arrays, io = {}, {}
    for short, name in _INS.items():
        a = np.ascontiguousarray(inputs[name])
        arrays[f"in_{short}"] = a
        io[short] = nc.dram_tensor(f"in_{short}", a.shape, mybir.dt.from_np(a.dtype), kind="ExternalInput").ap()
    io["out"] = nc.dram_tensor("out", [N, C], F32, kind="ExternalOutput").ap()
    graph_layers(nc, io)
    r = run_bass_kernel_spmd(nc, [arrays], core_ids=[0])
    return r.results[0]["out"]
```
